# Optimizing a Trainium2 kernel written in Bass

```python
import numpy as np
import jax
import jax.numpy as jnp

def _softmax(x, axis=-1):
    return jax.nn.softmax(x, axis=axis)

def _gelu(x):
    return jax.nn.gelu(x, approximate=True)

def _silu(x):
    return jax.nn.silu(x)

def _sigmoid(x):
    return jax.nn.sigmoid(x)

def _layernorm(x, axis=-1, eps=1e-05):
    m = jnp.mean(x, axis=axis, keepdims=True)
    v = jnp.var(x, axis=axis, keepdims=True)
    return (x - m) / jnp.sqrt(v + eps)

def _scatter_add(tgt, idx, src, axis=0):
    return tgt.at[idx].add(src)

def _segment_sum(src, seg, n):
    return jax.ops.segment_sum(src, seg, n)
kernel_name = 'mk_gnn_ffn_d1_gnn_r16_bedea1'

def setup_inputs(seed: int=0):
    np.random.seed(seed)
    _w = jnp.asarray

    def _rec_inputs():
        import jax
        import jax.numpy as jnp
        _gk = jax.random.key(seed)
        x = -0.0003019 + 1 * jax.random.normal(jax.random.fold_in(_gk, 1), (625, 1024), jnp.float32)
        src = jax.random.randint(jax.random.fold_in(_gk, 2), (10000,), 0, 625, jnp.int32)
        dst = jax.random.randint(jax.random.fold_in(_gk, 3), (10000,), 0, 625, jnp.int32)
        _o = jnp.argsort(dst, stable=True)
        src = src[_o]
        dst = dst[_o]
        return (x, src, dst)
    x, src, dst = _rec_inputs()

    def _L0_gnn_setup():
        import jax, jax.numpy as jnp
        import numpy as np
        N = 1250
        E = 20000
        D_IN = 1024
        D_OUT = 1024
        key = jax.random.key(seed)
        k1, k2, k3, k4 = jax.random.split(key, 4)
        x = jax.random.normal(k1, (N, D_IN), dtype=jnp.float32)
        edge_index = jax.random.randint(k2, (2, E), 0, N, dtype=jnp.int64)
        W = jax.random.normal(k3, (D_OUT, D_IN), dtype=jnp.float32) * (1.0 / np.sqrt(D_IN))
        b = jax.random.normal(k4, (D_OUT,), dtype=jnp.float32) * 0.01
        return {'x': x, 'edge_index': edge_index, 'W': W, 'b': b}
    _L0_gnn_all = _L0_gnn_setup()
    _L0_gnn_in = {k: v for k, v in _L0_gnn_all.items() if k in ('W', 'b')}
    del _L0_gnn_all

    def _L0_ffn_setup():
        import jax, jax.numpy as jnp
        import numpy as np
        B, S, D = (2, 128, 1024)
        E, K, H = (8, 4, 1024)
        SH = 2 * H

        def _silu(x):
            return x * jax.nn.sigmoid(x)

        def _swiglu(x, w1, b1, w2, b2):
            return _silu(x @ w1 + b1) * (x @ w2 + b2)

        def _moe(x, gate_w, exp_w1, exp_w3, exp_w2, sh_w1, sh_w3, sh_w2):
            b, s, d = x.shape
            t = b * s
            xt = x.reshape(t, d)
            scores = jax.nn.softmax(xt @ gate_w.T, axis=-1)
            topv, topi = jax.lax.top_k(scores, K)
            topv = topv / jnp.sum(topv, axis=-1, keepdims=True)
            combine = jnp.zeros((t, E), xt.dtype).at[jnp.arange(t)[:, None], topi].set(topv)
            g = _silu(jnp.einsum('td,edh->eth', xt, exp_w1))
            u = jnp.einsum('td,edh->eth', xt, exp_w3)
            yexp = jnp.einsum('eth,ehd->etd', g * u, exp_w2)
            routed = jnp.einsum('te,etd->td', combine, yexp)
            shared = _silu(xt @ sh_w1) * (xt @ sh_w3) @ sh_w2
            return (routed + shared).reshape(b, s, d)
        key = jax.random.key(seed)
        ks = jax.random.split(key, 24)
        f = lambda k, shape: jax.random.normal(k, shape, dtype=jnp.float32) * 0.02
        return {'x': jax.random.normal(ks[0], (B, S, D), dtype=jnp.float32), 'lin0_w': f(ks[1], (D, D)), 'lin0_b': f(ks[2], (D,)), 'swi1_w1': f(ks[3], (D, D)), 'swi1_b1': f(ks[4], (D,)), 'swi1_w2': f(ks[5], (D, D)), 'swi1_b2': f(ks[6], (D,)), 'gate_w': f(ks[7], (E, D)), 'exp_w1': f(ks[8], (E, D, H)), 'exp_w3': f(ks[9], (E, D, H)), 'exp_w2': f(ks[10], (E, H, D)), 'sh_w1': f(ks[11], (D, SH)), 'sh_w3': f(ks[12], (D, SH)), 'sh_w2': f(ks[13], (SH, D)), 'lin1_w': f(ks[14], (D, D)), 'lin1_b': f(ks[15], (D,)), 'swi2_w1': f(ks[16], (D, D)), 'swi2_b1': f(ks[17], (D,)), 'swi2_w2': f(ks[18], (D, D)), 'swi2_b2': f(ks[19], (D,))}
    _L0_ffn_all = _L0_ffn_setup()
    _L0_ffn_in = {k: v for k, v in _L0_ffn_all.items() if k in ('lin0_w', 'lin0_b', 'swi1_w1', 'swi1_b1', 'swi1_w2', 'swi1_b2', 'gate_w', 'exp_w1', 'exp_w3', 'exp_w2', 'sh_w1', 'sh_w3', 'sh_w2', 'lin1_w', 'lin1_b', 'swi2_w1', 'swi2_b1', 'swi2_w2', 'swi2_b2')}
    del _L0_ffn_all
    return {'x': x, 'src': src, 'dst': dst, 'L0_gnn_W': _L0_gnn_in['W'], 'L0_gnn_b': _L0_gnn_in['b'], 'L0_ffn_lin0_w': _L0_ffn_in['lin0_w'], 'L0_ffn_lin0_b': _L0_ffn_in['lin0_b'], 'L0_ffn_swi1_w1': _L0_ffn_in['swi1_w1'], 'L0_ffn_swi1_b1': _L0_ffn_in['swi1_b1'], 'L0_ffn_swi1_w2': _L0_ffn_in['swi1_w2'], 'L0_ffn_swi1_b2': _L0_ffn_in['swi1_b2'], 'L0_ffn_gate_w': _L0_ffn_in['gate_w'], 'L0_ffn_exp_w1': _L0_ffn_in['exp_w1'], 'L0_ffn_exp_w3': _L0_ffn_in['exp_w3'], 'L0_ffn_exp_w2': _L0_ffn_in['exp_w2'], 'L0_ffn_sh_w1': _L0_ffn_in['sh_w1'], 'L0_ffn_sh_w3': _L0_ffn_in['sh_w3'], 'L0_ffn_sh_w2': _L0_ffn_in['sh_w2'], 'L0_ffn_lin1_w': _L0_ffn_in['lin1_w'], 'L0_ffn_lin1_b': _L0_ffn_in['lin1_b'], 'L0_ffn_swi2_w1': _L0_ffn_in['swi2_w1'], 'L0_ffn_swi2_b1': _L0_ffn_in['swi2_b1'], 'L0_ffn_swi2_w2': _L0_ffn_in['swi2_w2'], 'L0_ffn_swi2_b2': _L0_ffn_in['swi2_b2']}

def reference(x, src, dst, L0_gnn_W, L0_gnn_b, L0_ffn_lin0_w, L0_ffn_lin0_b, L0_ffn_swi1_w1, L0_ffn_swi1_b1, L0_ffn_swi1_w2, L0_ffn_swi1_b2, L0_ffn_gate_w, L0_ffn_exp_w1, L0_ffn_exp_w3, L0_ffn_exp_w2, L0_ffn_sh_w1, L0_ffn_sh_w3, L0_ffn_sh_w2, L0_ffn_lin1_w, L0_ffn_lin1_b, L0_ffn_swi2_w1, L0_ffn_swi2_b1, L0_ffn_swi2_w2, L0_ffn_swi2_b2):
    import jax
    import jax.numpy as jnp

    def _L0_gnn_ref(x, edge_index, W, b):
        import jax, jax.numpy as jnp
        import numpy as np
        N = 1250
        E = 20000
        D_IN = 1024
        D_OUT = 1024
        num_nodes = x.shape[0]
        self_idx = jnp.arange(num_nodes, dtype=edge_index.dtype)
        ei = jnp.concatenate([edge_index, jnp.stack([self_idx, self_idx], axis=0)], axis=1)
        row, col = (ei[0], ei[1])
        h = jnp.einsum('nd,od->no', x, W) + b
        deg = jnp.zeros((num_nodes,), dtype=h.dtype).at[row].add(1.0)
        deg_inv_sqrt = deg ** (-0.5)
        norm = deg_inv_sqrt[row] * deg_inv_sqrt[col]
        msg = norm[:, None] * h[col]
        out = jax.ops.segment_sum(msg, row, num_segments=num_nodes)
        return out

    def _L0_ffn_ref(x, lin0_w, lin0_b, swi1_w1, swi1_b1, swi1_w2, swi1_b2, gate_w, exp_w1, exp_w3, exp_w2, sh_w1, sh_w3, sh_w2, lin1_w, lin1_b, swi2_w1, swi2_b1, swi2_w2, swi2_b2):
        import jax, jax.numpy as jnp
        import numpy as np
        B, S, D = (2, 128, 1024)
        E, K, H = (8, 4, 1024)
        SH = 2 * H

        def _silu(x):
            return x * jax.nn.sigmoid(x)

        def _swiglu(x, w1, b1, w2, b2):
            return _silu(x @ w1 + b1) * (x @ w2 + b2)

        def _moe(x, gate_w, exp_w1, exp_w3, exp_w2, sh_w1, sh_w3, sh_w2):
            b, s, d = x.shape
            t = b * s
            xt = x.reshape(t, d)
            scores = jax.nn.softmax(xt @ gate_w.T, axis=-1)
            topv, topi = jax.lax.top_k(scores, K)
            topv = topv / jnp.sum(topv, axis=-1, keepdims=True)
            combine = jnp.zeros((t, E), xt.dtype).at[jnp.arange(t)[:, None], topi].set(topv)
            g = _silu(jnp.einsum('td,edh->eth', xt, exp_w1))
            u = jnp.einsum('td,edh->eth', xt, exp_w3)
            yexp = jnp.einsum('eth,ehd->etd', g * u, exp_w2)
            routed = jnp.einsum('te,etd->td', combine, yexp)
            shared = _silu(xt @ sh_w1) * (xt @ sh_w3) @ sh_w2
            return (routed + shared).reshape(b, s, d)
        h = x @ lin0_w + lin0_b
        h = _swiglu(h, swi1_w1, swi1_b1, swi1_w2, swi1_b2)
        h = _moe(h, gate_w, exp_w1, exp_w3, exp_w2, sh_w1, sh_w3, sh_w2)
        h = h @ lin1_w + lin1_b
        h = _swiglu(h, swi2_w1, swi2_b1, swi2_w2, swi2_b2)
        return h
    edge_index = jnp.stack([src, dst])
    x = x + _L0_gnn_ref(_layernorm(x, axis=-1), edge_index, L0_gnn_W, L0_gnn_b)
    x = x + _L0_ffn_ref(_layernorm(x, axis=-1)[None], L0_ffn_lin0_w, L0_ffn_lin0_b, L0_ffn_swi1_w1, L0_ffn_swi1_b1, L0_ffn_swi1_w2, L0_ffn_swi1_b2, L0_ffn_gate_w, L0_ffn_exp_w1, L0_ffn_exp_w3, L0_ffn_exp_w2, L0_ffn_sh_w1, L0_ffn_sh_w3, L0_ffn_sh_w2, L0_ffn_lin1_w, L0_ffn_lin1_b, L0_ffn_swi2_w1, L0_ffn_swi2_b1, L0_ffn_swi2_w2, L0_ffn_swi2_b2)[0]
    return x

_drawn_inputs = setup_inputs


def setup_inputs(seed=0):
    import zlib

    import numpy as np

    out = dict(_drawn_inputs(seed))
    spreads = {}
    factors = {}
    for name, (base, spread) in spreads.items():
        noise = np.random.default_rng([zlib.crc32(name.encode()), seed]).standard_normal(out[name].shape)
        drawn = base * np.exp(spread * noise) if base else spread * noise
        out[name] = jnp.asarray(drawn.astype(out[name].dtype))
    for name, factor in factors.items():
        out[name] = (out[name] * factor).astype(out[name].dtype)
    return out
```

```python
import concourse.bass as bass
from concourse import mybir
from contextlib import ExitStack

T = 625
D = 1024
EDGES = 10000
EXPERTS = 8
TOP = 4
P = 128
KC = D // P
TT = 125
NT = T // TT
HT = 314
TP = 2 * HT
EC = EDGES // TT
GROUPS = (32, 32, 16)
CAP = 344
WIDTHS = (CAP - 48, CAP - 32, CAP - 24, CAP - 16, CAP)
SLOT_TILES = [(0, P), (P, P), (2 * P, CAP - 2 * P)]
RING = 4
OV_SLOTS = P
OV_ROUNDS = -(-(T - CAP) // OV_SLOTS)
OV_ALL = OV_ROUNDS * OV_SLOTS
UNITS_UP = 2 * KC
UNITS_EXPERT = 3 * KC

U_GNN = 0
U_LIN0 = U_GNN + KC
U_SWI1 = U_LIN0 + KC
U_SHA = U_SWI1 + UNITS_UP
U_EXP = U_SHA + UNITS_EXPERT
U_SHB = U_EXP + EXPERTS * UNITS_EXPERT
U_LIN1 = U_SHB + UNITS_EXPERT
U_SWI2 = U_LIN1 + KC
UNITS = U_SWI2 + UNITS_UP

B_LIN0, B_S1A, B_S1B, B_LIN1, B_S2A, B_S2B = range(6)


def build(nc, x, src, dst, gnn_b, biases, gate, stream, out):
    f32 = mybir.dt.float32
    f32r = mybir.dt.float32r
    f16 = mybir.dt.float16
    bf16 = mybir.dt.bfloat16
    i32 = mybir.dt.int32
    u32 = mybir.dt.uint32
    ALU = mybir.AluOpType
    ACT = mybir.ActivationFunctionType
    AX = mybir.AxisListType

    h_rows_dram = nc.dram_tensor("h_rows_dram", (T, D), f32).ap()
    y_dram = nc.dram_tensor("y_dram", (EXPERTS * CAP, D), f32).ap()
    ov_dram = nc.dram_tensor("ov_dram", (EXPERTS * OV_ALL, D), f32).ap()
    x1_dram = nc.dram_tensor("x1_dram", (T, D), f32).ap()

    ctx = ExitStack()
    with ctx:
        def sb(name, shape, dt):
            return ctx.enter_context(nc.sbuf_tensor(name, shape, dt))

        def sem(name):
            return ctx.enter_context(nc.semaphore(name))

        act_a = sb("act_a", [P, 2, NT * D], f32r)
        act_b = sb("act_b", [P, 2, KC * TP], f32r)
        act_x = sb("act_x", [P, 2, NT * TP], f32r)
        rows = sb("rows", [P, NT, D], f32)
        gath = sb("gath", [P, 3 * D + 68], f32)
        yrow = sb("yrow", [P, 3, D], f32)
        raw = sb("raw", [P, RING, D], f32)
        w_hi = sb("w_hi", [P, RING, D], f32r)
        w_lo = sb("w_lo", [P, RING, D], f32r)
        silu = sb("silu", [P, TP], f32)
        prod = sb("prod", [P, 2, TP], f32)
        ident = sb("ident", [P, P], f32)
        bias = sb("bias", [P, 6, KC], f32)
        stats = sb("stats", [P, NT, KC, 6], f32)
        sums = sb("sums", [P, 3, NT], f32)
        mv = sb("mv", [P, NT, 2], f32)
        rstd = sb("rstd", [P, NT], f32)
        dis = sb("dis", [P, NT], f32)
        brow = sb("brow", [P, NT], f32)
        ones = sb("ones", [P, 2], f32)
        lg = sb("lg", [P, NT, EXPERTS], f32)
        score = sb("score", [P, NT, EXPERTS], f32)
        rank = sb("rank", [P, NT, EXPERTS], f32)
        mask = sb("mask", [P, NT, EXPERTS], f32)
        mask16 = sb("mask16", [P, NT, EXPERTS], f16)
        slot = sb("slot", [P, NT, EXPERTS], f32)
        ykey = sb("ykey", [P, NT, EXPERTS], f32)
        pick = sb("pick", [P, NT, EXPERTS], f32)
        col1 = sb("col1", [P, NT], f32)
        top_row = sb("top_row", [P, TOP, NT], f32)
        top_idx = sb("top_idx", [P, TOP, NT], u32)
        top_w = sb("top_w", [P, TOP, NT], f32)
        used_i = sb("used_i", [P, EXPERTS], i32)
        most = sb("most", [P, 1], f32)
        most_i = sb("most_i", [P, 1], i32)
        ov_idx = sb("ov_idx", [P, TOP, NT], u32)
        ov_w = sb("ov_w", [P, TOP, NT], f32)
        tok_id = sb("tok_id", [P, NT], f16)
        slot_tok = sb("slot_tok", [P, EXPERTS * 3], u32)
        now_tok = sb("now_tok", [P, 3], u32)

        acc = ctx.enter_context(nc.psum_tensor("acc", [P, 8, 512], f32))
        TPB = 4

        def hl(t, n, w):
            return [t[:, s, 0:n * w].rearrange("p (k w) -> p k w", w=w) for s in range(2)]

        a_hi, a_lo = hl(act_a, KC, TP)
        b_hi, b_lo = hl(act_b, KC, TP)
        e_hi, e_lo = hl(act_x, KC, CAP)
        g_hi, g_lo = hl(act_b, KC, CAP)
        xs_hi, xs_lo = hl(act_a, NT, D)
        c_hi, c_lo = hl(act_x, NT, TP)
        counts = gath[:, 0:NT * TP].rearrange("p (i w) -> p i w", w=TP)
        grow = gath[:, 0:3 * D].rearrange("p (s d) -> p s d", d=D)
        gate_raw = gath[:, 0:D]
        gate_hi = act_x[:, 0, 0:D]
        gate_lo = act_x[:, 1, 0:D]
        logits_t = gath[0:EXPERTS, D:D + TP]
        yr = yrow[:, :, :].rearrange("p s d -> p (s d)")
        scratch16 = yr.bitcast(bf16)
        OHR = 4
        oh_dst = scratch16[:, 0:OHR * 626].rearrange("p (s w) -> p s w", w=626)
        oh_src = scratch16[:, OHR * 626:OHR * 626 + OHR * HT].rearrange("p (s w) -> p s w", w=HT)
        onehot = yr.bitcast(f16)[:, 0:2 * NT * CAP].rearrange("p (e i c) -> p e i c", e=2, i=NT)
        iota = yr.bitcast(f16)[:, 3776:3776 + TP]
        tri = yr.bitcast(f16)[:, 4416:4416 + TT]
        full16 = yr.bitcast(f16)[:, 4544:4544 + P]
        lower = yr[:, 2336:2336 + 64].rearrange("p (e j) -> p e j", j=EXPERTS)
        cmp_gt = yr[:, 2400:2400 + 320].rearrange("p (i e j) -> p i e j", i=NT, e=EXPERTS)
        cmp_eq = yr[:, 2720:2720 + 320].rearrange("p (i e j) -> p i e j", i=NT, e=EXPERTS)
        pw = prod[:, :, :].rearrange("p s w -> p (s w)")
        dst_f = pw[:, 0:EC]
        src_f = pw[:, EC:2 * EC]
        src_m = pw[:, 2 * EC:3 * EC]
        src_v = pw[:, 3 * EC:4 * EC]
        idx_i = pw[:, 4 * EC:6 * EC].bitcast(i32)
        upper_i = [silu[:, 0:HT].bitcast(i32), pw[:, 6 * EC:6 * EC + HT].bitcast(i32)]
        lower_c = silu[:, HT:2 * HT]
        zeros = pw[:, 800:800 + HT // 2].bitcast(bf16)
        gnn_bb = yr[:, 0:D]

        def acc_dense(s):
            return acc[:, 2 * s:2 * s + 2, 0:HT]

        def halves(t):
            return t.rearrange("p (h n) -> p h n", h=2)

        def back_slot(k):
            return grow[0:TT, k, :] if k < 3 else yrow[0:TT, 0, :]

        def sum_slot(i):
            return yrow[0:TT, 1 + i % 2, :]

        def count_bank(g, i):
            return (NT * g + i) % 8

        def ysum(m):
            return rows[:, :, :].rearrange("p i d -> p (i d)")[:, m * TP:(m + 1) * TP]

        raw_loaded = [sem(f"raw_loaded{s}") for s in range(RING)]
        hi_split = sem("hi_split")
        lo_split = sem("lo_split")
        unit_done = sem("unit_done")
        const_ready = sem("const_ready")
        ident_zero = sem("ident_zero")
        tri_set = sem("tri_set")
        idx_loaded = sem("idx_loaded")
        x_loaded = sem("x_loaded")
        small_loaded = sem("small_loaded")
        onehot_ready = sem("onehot_ready")
        onehot_used = sem("onehot_used")
        counts_done = sem("counts_done")
        counts_read = sem("counts_read")
        banks_read = sem("banks_read")
        gnn_b_loaded = sem("gnn_b_loaded")
        counts_hi = sem("counts_hi")
        counts_lo = sem("counts_lo")
        deg_done = sem("deg_done")
        deg_root = sem("deg_root")
        dis_ready = sem("dis_ready")
        sums_done = sem("sums_done")
        act_chain = sem("act_chain")
        squares_ready = sem("squares_ready")
        var_ready = sem("var_ready")
        shift_ready = sem("shift_ready")
        root_ready = sem("root_ready")
        xn_ready = sem("xn_ready")
        xs_hi_ready = sem("xs_hi_ready")
        xs_lo_ready = sem("xs_lo_ready")
        x_again = sem("x_again")
        z_done = sem("z_done")
        z_hi = sem("z_hi")
        z_lo = sem("z_lo")
        gnn_copy = sem("gnn_copy")
        gnn_tp = sem("gnn_tp")
        gnn_x1 = sem("gnn_x1")
        ln_var = sem("ln_var")
        ln_root = sem("ln_root")
        ln_rows = sem("ln_rows")
        ln_tp = sem("ln_tp")
        ln_hi = sem("ln_hi")
        ln_lo = sem("ln_lo")
        pads_zero = sem("pads_zero")
        x1_saved = sem("x1_saved")
        x1_back = sem("x1_back")
        dve_chain = sem("dve_chain")
        chain = [dve_chain, 0]
        out_saved = sem("out_saved")

        class Stage:
            def __init__(self, name, base):
                self.base = base
                self.silu = sem(name + "_silu")
                self.prod = sem(name + "_prod")
                self.hi = sem(name + "_hi")
                self.lo = sem(name + "_lo")

        lin0 = Stage("lin0", U_LIN0)
        swi1 = Stage("swi1", U_SWI1)
        sha = Stage("sha", U_SHA)
        exp = Stage("exp", U_EXP)
        shb = Stage("shb", U_SHB)
        lin1 = Stage("lin1", U_LIN1)
        swi2 = Stage("swi2", U_SWI2)
        sha_y = sem("sha_y")
        shb_sum = sem("shb_sum")
        shb_dhi = sem("shb_dhi")
        shb_dlo = sem("shb_dlo")
        h_tp = sem("h_tp")
        h_copied = sem("h_copied")
        h_saved = sem("h_saved")
        gate_split = sem("gate_split")
        gate_loaded = sem("gate_loaded")
        logits_summed = sem("logits_summed")
        logits_copied = sem("logits_copied")
        logits_done = sem("logits_done")
        shifted = sem("shifted")
        exped = sem("exped")
        mask_ready = sem("mask_ready")
        slots_done = sem("slots_done")
        routed = sem("routed")
        oh_ready = sem("oh_ready")
        tok_done = sem("tok_done")
        tok_copied = sem("tok_copied")
        gathered = sem("gathered")
        now_ready = sem("now_ready")
        gather_go = sem("gather_go")
        save_go = sem("save_go")
        xe_tp = sem("xe_tp")
        xe_hi = sem("xe_hi")
        xe_lo = sem("xe_lo")
        yt_copied = sem("yt_copied")
        y_tp = sem("y_tp")
        y_copied = sem("y_copied")
        y_saved = sem("y_saved")
        back = [sem(f"back{s}") for s in range(TOP)]
        back_used = sem("back_used")
        sum_tp = sem("sum_tp")
        sum_used = sem("sum_used")
        o_tp = sem("o_tp")
        o_rows = sem("o_rows")

        ov_iota = yr.bitcast(f16)[:, 2 * D:2 * D + OV_ALL]
        ov_onehot = yr.bitcast(f16)[:, 4 * D:4 * D + NT * OV_SLOTS].rearrange("p (i c) -> p i c", i=NT)
        ov_in = grow[:, 0, :]
        ov_raw = grow[:, 1, :]
        ov_out = yrow[:, 0, :]
        OVS = RING - 1
        ov_ready = sem("ov_ready")
        ov_oh = sem("ov_oh")
        ov_tok = sem("ov_tok")
        ov_tok_copied = sem("ov_tok_copied")
        ov_go = sem("ov_go")
        ov_gathered = sem("ov_gathered")
        ov_xt = sem("ov_xt")
        ov_xhi = sem("ov_xhi")
        ov_xlo = sem("ov_xlo")
        ov_loaded = sem("ov_loaded")
        ov_hi = sem("ov_hi")
        ov_lo = sem("ov_lo")
        ov_unit = sem("ov_unit")
        ov_silu = sem("ov_silu")
        ov_prod = sem("ov_prod")
        ov_ghi = sem("ov_ghi")
        ov_glo = sem("ov_glo")
        ov_yt = sem("ov_yt")
        ov_yx = sem("ov_yx")
        ov_y = sem("ov_y")
        ov_saved = sem("ov_saved")
        ov_chain = sem("ov_chain")
        ov_routed = sem("ov_routed")
        ov_back = sem("ov_back")
        ov_used = sem("ov_used")
        ov_sum = sem("ov_sum")
        ov_added = sem("ov_added")

        def fullest(eng):
            eng.wait_ge(routed, 1)
            return eng.value_load(most_i[0:1, 0:1], min_val=0, max_val=T)

        block = ctx.enter_context(nc.Block())

        @block.sync
        def _(sp):
            sp.dma_start(idx_i[0:TT, 0:EC], dst).then_inc(idx_loaded, 16)
            sp.dma_start(idx_i[0:TT, EC:2 * EC], src).then_inc(idx_loaded, 16)
            sp.dma_start(rows[0:TT, :, :], x.rearrange("(i p) d -> p i d", p=TT)).then_inc(x_loaded, 16)
            for s in range(RING):
                sp.dma_start(raw[:, s, :], stream[s, :, :]).then_inc(raw_loaded[s], 16)
            sp.dma_start(bias[:, :, :], biases).then_inc(small_loaded, 16)
            with sp.Fori(1, UNITS // RING) as g:
                for s in range(RING):
                    sp.wait_ge(hi_split, g * RING + (s + 1 - RING))
                    sp.wait_ge(lo_split, g * RING + (s + 1 - RING))
                    sp.dma_start(raw[:, s, :],
                                 stream[bass.ds(g * RING + s, 1), :, :].rearrange("u p n -> (u p) n")
                                 ).then_inc(raw_loaded[s], 16)

        def arrived(eng, u, off):
            s = off % RING
            if isinstance(u, int):
                eng.wait_ge(raw_loaded[s], 16 * ((u + off) // RING + 1))
                if u + off >= RING:
                    eng.wait_ge(unit_done, u + off - RING + 1)
            else:
                eng.wait_ge(raw_loaded[s], u * (16 // RING) + 16 * (off // RING + 1))
                eng.wait_ge(unit_done, u + (off - RING + 1))
            return s

        def split_hi(u, off):
            s = arrived(nc.scalar, u, off)
            nc.scalar.activation(w_hi[:, s, :], raw[:, s, :], ACT.Copy).then_inc(hi_split, 1)

        def split_lo(u, off):
            s = arrived(nc.gpsimd, u, off)
            if isinstance(u, int):
                nc.gpsimd.wait_ge(hi_split, u + off + 1)
            else:
                nc.gpsimd.wait_ge(hi_split, u + (off + 1))
            nc.gpsimd.tensor_tensor(w_lo[:, s, :], raw[:, s, :], w_hi[:, s, :].bitcast(f32),
                                    ALU.subtract).then_inc(lo_split, 1)

        @block.gpsimd
        def _(pool):
            pool.iota(iota[:, :], [[1, TP]], base=0, channel_multiplier=0,
                      allow_small_or_imprecise_dtypes=True).then_inc(const_ready, 1)
            pool.iota(tok_id[:, :], [[TT, NT]], base=0, channel_multiplier=1,
                      allow_small_or_imprecise_dtypes=True).then_inc(const_ready, 1)
            pool.memset(zeros[:, :], 0.0).then_inc(const_ready, 1)
            pool.memset(ones[:, :], 1.0).then_inc(const_ready, 1)
            pool.memset(ident[:, :], 0.0).then_inc(ident_zero, 1)
            pool.wait_ge(ident_zero, 1)
            pool.affine_select(out=ident[:, :], in_=ident[:, :], compare_op=ALU.not_equal, fill=1.0, base=0,
                               pattern=[[-1, P]], channel_multiplier=1).then_inc(const_ready, 1)
            pool.memset(slot_tok[:, :], 0).then_inc(const_ready, 1)
            for o in range(3):
                split_lo(0, o)
            for m in range(KC):
                split_lo(U_GNN, m + 3)
            pool.wait_ge(counts_done, 3)
            pool.memset(tri[0:TT, :], 1.0).then_inc(tri_set, 1)
            pool.memset(full16[:, :], 1.0).then_inc(tri_set, 1)
            pool.memset(lower[:, :, :], 1.0).then_inc(tri_set, 1)
            pool.wait_ge(tri_set, 3)
            pool.affine_select(out=tri[0:TT, :], in_=tri[0:TT, :], compare_op=ALU.is_gt, fill=0.0, base=0,
                               pattern=[[1, TT]], channel_multiplier=-1).then_inc(tri_set, 1)
            pool.affine_select(out=lower[:, :, :], in_=lower[:, :, :], compare_op=ALU.is_gt, fill=0.0,
                               base=0, pattern=[[1, EXPERTS], [-1, EXPERTS]],
                               channel_multiplier=0).then_inc(tri_set, 1)
            for u in range(U_LIN0, U_SHA):
                split_lo(u // RING * RING, u % RING + 3)

            def gather(e):
                pool.tensor_copy(now_tok[:, :], slot_tok[:, bass.ds(3 * e, 3)]).then_inc(now_ready, 1)
                pool.wait_ge(h_saved, 16)
                pool.wait_ge(now_ready, e + 1)
                pool.sem_inc(gather_go, 1)
                for n, (c0, cn) in enumerate(SLOT_TILES):
                    pool.indirect_dma_start(out=grow[0:cn, n, :], out_offset=None, in_=h_rows_dram,
                                            in_offset=bass.IndirectOffsetOnAxis(ap=now_tok[0:cn, n:n + 1], axis=0)
                                            ).then_inc(gathered, 16)

            for j in range(UNITS_EXPERT):
                if j == 12:
                    pool.wait_ge(routed, 1)
                    pool.wait_ge(tok_copied, 1)
                    pool.wait_ge(ln_tp, 2 * NT)
                    gather(0)
                split_lo(U_SHA, j + 3)
            pool.wait_ge(tok_copied, 4)

            def save_y(e):
                pool.wait_ge(y_copied, e * KC + KC)
                pool.sem_inc(save_go, 1)
                for n, (c0, cn) in enumerate(SLOT_TILES):
                    pool.dma_start(y_dram[bass.ds(e * CAP + c0, cn), :],
                                   yrow[0:cn, n, :]).then_inc(y_saved, 16)

            pool.wait_ge(xe_tp, KC)
            gather(1)
            for j in range(UNITS_EXPERT):
                split_lo(U_EXP, j + 3)
            with pool.Fori(1, EXPERTS - 1) as e:
                save_y(e - 1)
                pool.wait_ge(xe_tp, e * KC + KC)
                gather(e + 1)
                for j in range(UNITS_EXPERT):
                    split_lo(e * UNITS_EXPERT + U_EXP, j + 3)
            save_y(EXPERTS - 2)
            for j in range(UNITS_EXPERT):
                split_lo(U_SHB - UNITS_EXPERT, j + 3)
            save_y(EXPERTS - 1)

            with pool.If(fullest(pool) > CAP):
                pool.wait_ge(y_saved, 16 * 3 * EXPERTS)
                pool.wait_ge(xe_tp, EXPERTS * KC)
                pool.iota(ov_iota, [[1, OV_ALL]], base=CAP, channel_multiplier=0,
                          allow_small_or_imprecise_dtypes=True).then_inc(ov_ready, 1)
                with pool.Fori(0, OV_ROUNDS) as c:
                    with pool.Fori(0, EXPERTS) as e:
                        n = c * EXPERTS + e
                        pool.wait_ge(ov_tok_copied, n + 1)
                        pool.sem_inc(ov_go, 1)
                        pool.indirect_dma_start(out=ov_in, out_offset=None, in_=h_rows_dram,
                                                in_offset=bass.IndirectOffsetOnAxis(ap=now_tok[:, 0:1], axis=0)
                                                ).then_inc(ov_gathered, 16)
                        pool.wait_ge(ov_y, n * KC + KC)
                        pool.sem_inc(ov_go, 1)
                        pool.dma_start(ov_dram[bass.ds(e * OV_ALL + c * OV_SLOTS, OV_SLOTS), :],
                                       ov_out).then_inc(ov_saved, 16)
                        pool.wait_ge(ov_saved, n * 16 + 16)
                        pool.sem_inc(ov_go, 1)
                pool.wait_ge(ov_routed, 1)
                for n in range(NT * TOP):
                    i, k = divmod(n, TOP)
                    if n >= 1:
                        pool.wait_ge(ov_used, n)
                    pool.indirect_dma_start(out=ov_in[0:TT, :], out_offset=None, in_=ov_dram,
                                            in_offset=bass.IndirectOffsetOnAxis(ap=ov_idx[0:TT, k, i:i + 1], axis=0)
                                            ).then_inc(ov_back, 16)
                pool.wait_ge(ov_added, 2 * NT)

            pool.wait_ge(y_saved, 16 * 3 * EXPERTS)
            pool.wait_ge(xe_tp, EXPERTS * KC)
            for j in range(UNITS_EXPERT):
                split_lo(U_SHB, j + 3)
                if j % 2 == 1 and j // 2 < NT:
                    i = j // 2
                    for k in range(TOP):
                        if i >= 1:
                            pool.wait_ge(back_used, TOP * (i - 1) + k + 1)
                        pool.indirect_dma_start(out=back_slot(k), out_offset=None, in_=y_dram,
                                                in_offset=bass.IndirectOffsetOnAxis(
                                                    ap=top_idx[0:TT, k, i:i + 1], axis=0)
                                                ).then_inc(back[k], 16)
            for u in range(U_LIN1, UNITS):
                if u + 3 < UNITS:
                    split_lo(u // RING * RING, u % RING + 3)

        @block.scalar
        def _(act):
            for o in range(3):
                split_hi(0, o)
            act.wait_ge(x_loaded, 16)
            for i in range(NT):
                ins = act.activation(xs_hi[0:TT, i, :], rows[0:TT, i, :], ACT.Copy, scale=-1.0 / D,
                                     accum_out=sums[0:TT, 0, i:i + 1])
            ins.then_inc(act_chain, 1)
            act.wait_ge(act_chain, 1)
            for i in range(NT):
                ins = act.activation(xs_hi[0:TT, i, :], rows[0:TT, i, :], ACT.Square, bias=sums[0:TT, 0, i:i + 1],
                                     accum_out=sums[0:TT, 1, i:i + 1])
            ins.then_inc(squares_ready, 1)
            act.wait_ge(var_ready, 1)
            act.activation(rstd[0:TT, :], mv[0:TT, :, 1], ACT.Sqrt).then_inc(root_ready, 1)
            act.wait_ge(shift_ready, 1)
            for i in range(NT):
                act.activation(rows[0:TT, i, :], rows[0:TT, i, :], ACT.Identity, scale=rstd[0:TT, i:i + 1],
                               bias=sums[0:TT, 2, i:i + 1]).then_inc(xn_ready, 1)
            for i in range(NT):
                act.wait_ge(counts_read, i + 1)
                act.activation(c_hi[0:TT, i, :], counts[0:TT, i, :], ACT.Copy).then_inc(counts_hi, 1)
            act.dma_start(gnn_bb[0:TT, :], gnn_b.partition_broadcast(TT)).then_inc(gnn_b_loaded, 16)
            act.wait_ge(deg_done, 1)
            act.activation(dis[0:TT, :], acc[0:TT, 0, 0:NT], ACT.Sqrt).then_inc(deg_root, 1)
            act.wait_ge(dis_ready, 1)
            act.wait_ge(xn_ready, NT)
            for i in range(NT):
                act.activation(xs_hi[0:TT, i, :], rows[0:TT, i, :], ACT.Copy,
                               scale=dis[0:TT, i:i + 1]).then_inc(xs_hi_ready, 1)
            act.wait_ge(xs_lo_ready, NT)
            act.dma_start(rows[0:TT, :, :], x.rearrange("(i p) d -> p i d", p=TT)).then_inc(x_again, 16)
            for m in range(KC):
                act.wait_ge(z_done, m + 1)
                act.activation(halves(b_hi[:, m, :]), acc_dense(m % 2), ACT.Copy).then_inc(z_hi, 1)
            for m in range(KC):
                split_hi(U_GNN, m + 3)
                act.wait_ge(unit_done, U_GNN + m + 1)
                if m >= 2:
                    act.wait_ge(gnn_tp, m - 1)
                act.activation(halves(prod[:, m % 2, :]), acc_dense(m % 2), ACT.Copy).then_inc(gnn_copy, 1)
            act.wait_ge(ln_var, 1)
            act.activation(rstd[0:TT, :], mv[0:TT, :, 1], ACT.Sqrt).then_inc(ln_root, 1)
            for i in range(NT):
                for q in range(2):
                    act.wait_ge(ln_tp, 2 * i + q + 1)
                    act.activation(a_hi[:, 4 * q:4 * q + 4, i * TT:(i + 1) * TT],
                                   acc[:, TPB + (2 * i + q) % 4, 0:500].rearrange("p (k t) -> p k t", k=4),
                                   ACT.Copy).then_inc(ln_hi, 1)
            act.wait_ge(gnn_x1, KC)
            act.dma_start(x1_dram.rearrange("(i p) d -> p i d", p=TT), rows[0:TT, :, :]).then_inc(x1_saved, 16)
            act.dma_start(gate_raw, gate).then_inc(gate_loaded, 16)
            act.wait_ge(small_loaded, 16)

            def linear_hi(st, o_hi, b):
                for m in range(KC):
                    split_hi(st.base, m + 3)
                    act.wait_ge(unit_done, st.base + m + 1)
                    act.activation(halves(o_hi[:, m, :]), acc_dense(m % 2), ACT.Identity,
                                   bias=bias[:, b, m:m + 1]).then_inc(st.hi, 1)

            def gated_pair(st, m, o_hi, b, last=False):
                if st.base + 2 * m + 3 < UNITS:
                    split_hi(st.base, 2 * m + 3)
                act.wait_ge(unit_done, st.base + 2 * m + 1)
                if m >= 1:
                    act.wait_ge(st.prod, m)
                kw = {} if b is None else {"bias": bias[:, b, m:m + 1]}
                act.activation(halves(silu[:, :]), acc_dense(0), ACT.Silu, **kw).then_inc(st.silu, 1)
                if st.base + 2 * m + 4 < UNITS:
                    split_hi(st.base, 2 * m + 4)
                if o_hi is not None:
                    act.wait_ge(st.prod, m + 1)
                    act.activation(o_hi[:, m, :], prod[:, m % 2, :], ACT.Copy).then_inc(st.hi, 1)

            linear_hi(lin0, b_hi, B_LIN0)
            act.wait_ge(gate_loaded, 16)
            act.activation(gate_hi, gate_raw, ACT.Copy).then_inc(gate_split, 1)
            for m in range(KC):
                gated_pair(swi1, m, a_hi, B_S1A)
            act.wait_ge(h_copied, KC)
            act.dma_start(h_rows_dram.rearrange("(i p) d -> p i d", p=TT), rows[0:TT, :, :]).then_inc(h_saved, 16)
            for m in range(KC):
                gated_pair(sha, m, b_hi, None)
                if m == 1:
                    act.wait_ge(shifted, 1)
                    act.activation(score[0:TT, :, :], lg[0:TT, :, :], ACT.Exp).then_inc(exped, 1)

            def expert_in_hi(e, m):
                act.wait_ge(xe_tp, e * KC + (m + 1))
                act.activation(e_hi[:, m, :], acc[:, TPB + 2 + m % 2, 0:CAP], ACT.Copy).then_inc(xe_hi, 1)

            for m in range(KC):
                split_hi(U_SHA + UNITS_UP, m + 3)
                act.wait_ge(unit_done, U_SHA + UNITS_UP + m + 1)
                if m == 0:
                    act.wait_ge(h_saved, 16)
                act.activation(halves(ysum(m)), acc_dense(m % 2), ACT.Copy).then_inc(sha_y, 1)
                expert_in_hi(0, m)

            def expert(e, nxt):
                base = e * UNITS_EXPERT + U_EXP
                for m in range(KC):
                    split_hi(base, 2 * m + 3)
                    act.wait_ge(unit_done, base + (2 * m + 1))
                    if m >= 1:
                        act.wait_ge(exp.prod, e * KC + m)
                    act.activation(silu[:, 0:CAP], acc[:, 2 * m % 4, 0:CAP], ACT.Silu).then_inc(exp.silu, 1)
                    split_hi(base, 2 * m + 4)
                    act.wait_ge(exp.prod, e * KC + (m + 1))
                    act.activation(g_hi[:, m, :], prod[:, m % 2, 0:CAP], ACT.Copy).then_inc(exp.hi, 1)
                for m in range(KC):
                    split_hi(base, UNITS_UP + m + 3)
                    act.wait_ge(unit_done, base + (UNITS_UP + m + 1))
                    if m >= 2:
                        act.wait_ge(y_tp, e * KC + (m - 1))
                    act.activation(prod[:, m % 2, 0:CAP], acc[:, m % 4, 0:CAP], ACT.Copy).then_inc(yt_copied, 1)
                    if nxt:
                        expert_in_hi(e + 1, m)

            with act.Fori(0, EXPERTS - 1) as e:
                expert(e, True)
            expert(EXPERTS - 1, False)

            with act.If(fullest(act) > CAP):
                act.wait_ge(y_tp, EXPERTS * KC)
                with act.Fori(0, OV_ROUNDS) as c:
                    with act.Fori(0, EXPERTS) as e:
                        n = c * EXPERTS + e

                        def load_unit(j, count):
                            act.dma_start(ov_raw, stream[bass.ds(e * UNITS_EXPERT + U_EXP + j, 1), :, :]
                                          .rearrange("u p n -> (u p) n")).then_inc(ov_loaded, 16)
                            act.wait_ge(ov_loaded, count * 16 + 16)
                            act.activation(w_hi[:, OVS, :], ov_raw, ACT.Copy).then_inc(ov_hi, 1)
                            act.wait_ge(ov_unit, count + 1)

                        act.wait_ge(ov_xt, n + 1)
                        for q in range(2):
                            act.activation(e_hi[:, 4 * q:4 * q + 4, 0:OV_SLOTS],
                                           acc[:, TPB + 1 + q, :].rearrange("p (k t) -> p k t", k=4),
                                           ACT.Copy).then_inc(ov_xhi, 1)
                        with act.Fori(0, KC) as m:
                            load_unit(m * 2, n * UNITS_EXPERT + m * 2)
                            load_unit(m * 2 + 1, n * UNITS_EXPERT + m * 2 + 1)
                            act.activation(silu[:, 0:OV_SLOTS], acc[:, 0, 0:OV_SLOTS], ACT.Silu).then_inc(ov_silu, 1)
                            act.wait_ge(ov_prod, n * KC + m + 1)
                            act.activation(g_hi[:, bass.ds(m, 1), 0:OV_SLOTS].rearrange("p m t -> p (m t)"),
                                           prod[:, 0, 0:OV_SLOTS], ACT.Copy).then_inc(ov_ghi, 1)
                        with act.Fori(0, KC) as m:
                            load_unit(m + UNITS_UP, n * UNITS_EXPERT + m + UNITS_UP)
                            act.activation(prod[:, 1, 0:OV_SLOTS], acc[:, 0, 0:OV_SLOTS], ACT.Copy).then_inc(ov_yt, 1)
                act.wait_ge(ov_added, 2 * NT)

            for m in range(KC):
                gated_pair(shb, m, b_hi, None)
            for m in range(KC):
                split_hi(U_SHB + UNITS_UP, m + 3)
                act.wait_ge(shb_sum, m + 1)
                act.activation(a_hi[:, m, :], prod[:, m % 2, :], ACT.Copy).then_inc(shb_dhi, 1)
            act.dma_start(rows[0:TT, :, :], x1_dram.rearrange("(i p) d -> p i d", p=TT)).then_inc(x1_back, 16)
            linear_hi(lin1, b_hi, B_LIN1)
            for m in range(KC):
                gated_pair(swi2, m, None, B_S2A)
                if m in (4, 6):
                    c0, c1 = (0, 4 * P) if m == 4 else (4 * P, 6 * P)
                    act.wait_ge(o_rows, c1 // P)
                    act.dma_start(out.rearrange("(i p) d -> p i d", p=TT)[:, :, c0:c1],
                                  rows[0:TT, :, c0:c1]).then_inc(out_saved, 16)
            act.wait_ge(o_rows, KC)
            act.dma_start(out.rearrange("(i p) d -> p i d", p=TT)[:, :, 6 * P:D],
                          rows[0:TT, :, 6 * P:D]).then_inc(out_saved, 16)
            act.wait_ge(out_saved, 48)
            act.wait_ge(x1_saved, 16)

        @block.vector
        def _(dve):
            def link(ins):
                chain[1] += 1
                ins.then_inc(chain[0], 1)
                dve.wait_ge(chain[0], chain[1])

            dve.wait_ge(idx_loaded, 32)
            dve.tensor_copy(dst_f[0:TT, :], idx_i[0:TT, 0:EC])
            link(dve.tensor_copy(src_f[0:TT, :], idx_i[0:TT, EC:2 * EC]))
            link(dve.tensor_scalar(src_v[0:TT, :], src_f[0:TT, :], float(HT), None, ALU.is_ge))
            link(dve.scalar_tensor_tensor(out=src_m[0:TT, :], in0=src_v[0:TT, :], scalar=-float(HT),
                                          in1=src_f[0:TT, :], op0=ALU.mult, op1=ALU.add))
            link(dve.tensor_scalar(src_v[0:TT, :], src_v[0:TT, :], 4095.0, 1.0, ALU.mult, ALU.add))
            dve.wait_ge(const_ready, 6)

            def onehots(j, s):
                dve.tensor_scalar(oh_dst[0:TT, s, 0:T], iota[0:TT, 0:T], dst_f[0:TT, j], None, ALU.is_equal)
                dve.tensor_scalar(oh_src[0:TT, s, :], iota[0:TT, 0:HT], src_m[0:TT, j], src_v[0:TT, j],
                                  ALU.is_equal, ALU.mult).then_inc(onehot_ready, 1)

            def iteration(it):
                for s in range(OHR):
                    if isinstance(it, int):
                        if it >= 1:
                            dve.wait_ge(onehot_used, it * OHR + s + 1 - OHR)
                        onehots(slice(it * OHR + s, it * OHR + s + 1), s)
                    else:
                        dve.wait_ge(onehot_used, it * OHR + (s + 1 - OHR))
                        onehots(bass.ds(it * OHR + s, 1), s)

            def decode(g, i):
                if i == 0:
                    dve.wait_ge(counts_done, g + 1)
                v = acc[0:TT, count_bank(g, i), 0:HT]
                upper = upper_i[i % 2][0:TT, :]
                low, high = counts[0:TT, i, 0:HT], counts[0:TT, i, HT:TP]
                link(dve.tensor_scalar(upper, v, 1.0 / 4096, -0.5 + 2.0 ** -13, ALU.mult, ALU.add))
                if g == 0:
                    dve.scalar_tensor_tensor(out=low, in0=upper, scalar=-4096.0, in1=v,
                                             op0=ALU.mult, op1=ALU.add).then_inc(banks_read, 1)
                    link(dve.tensor_copy(high, upper))
                    own = counts[0:TT, i, i * TT:(i + 1) * TT]
                    link(dve.tensor_tensor(own, own, ident[0:TT, 0:TT], ALU.add))
                else:
                    dve.scalar_tensor_tensor(out=lower_c[0:TT, :], in0=upper, scalar=-4096.0,
                                             in1=v, op0=ALU.mult, op1=ALU.add).then_inc(banks_read, 1)
                    dve.wait_ge(banks_read, NT * g + i + 1)
                    dve.tensor_tensor(low, low, lower_c[0:TT, :], ALU.add)
                    last = dve.tensor_tensor(high, high, upper, ALU.add)
                    if g == len(GROUPS) - 1:
                        last.then_inc(counts_read, 1)
                    else:
                        link(last)

            iteration(0)
            with dve.Fori(1, GROUPS[0] // OHR) as it:
                iteration(it)
            at = GROUPS[0] // OHR
            for g in range(1, len(GROUPS)):
                iteration(at)
                decode(g - 1, 0)
                decode(g - 1, 1)
                for i in range(2, NT):
                    iteration(at + i - 1)
                    decode(g - 1, i)
                done, at = at + NT - 1, at + GROUPS[g] // OHR
                if g == 1:
                    dve.wait_ge(squares_ready, 1)
                    dve.tensor_scalar(mv[0:TT, :, 1], sums[0:TT, 1, :], 1.0 / D, 1e-5, ALU.mult,
                                      ALU.add).then_inc(var_ready, 1)
                if done < at:
                    with dve.Fori(done, at) as it:
                        iteration(it)
                if g == 1:
                    dve.wait_ge(root_ready, 1)
                    link(dve.reciprocal(rstd[0:TT, :], rstd[0:TT, :]))
                    dve.tensor_tensor(sums[0:TT, 2, :], sums[0:TT, 0, :], rstd[0:TT, :],
                                      ALU.mult).then_inc(shift_ready, 1)
            for i in range(NT):
                decode(len(GROUPS) - 1, i)
            for i in range(NT):
                dve.wait_ge(counts_hi, i + 1)
                dve.tensor_tensor(c_lo[0:TT, i, :], counts[0:TT, i, :], c_hi[0:TT, i, :].bitcast(f32),
                                  ALU.subtract).then_inc(counts_lo, 1)
            dve.wait_ge(deg_root, 1)
            dve.reciprocal(dis[0:TT, :], dis[0:TT, :]).then_inc(dis_ready, 1)
            dve.wait_ge(dis_ready, 1)
            for i in range(NT):
                dve.wait_ge(xs_hi_ready, i + 1)
                dve.scalar_tensor_tensor(out=xs_lo[0:TT, i, :], in0=rows[0:TT, i, :], scalar=dis[0:TT, i:i + 1],
                                         in1=xs_hi[0:TT, i, :].bitcast(f32), op0=ALU.mult,
                                         op1=ALU.subtract).then_inc(xs_lo_ready, 1)
            dve.wait_ge(sums_done, 1)
            link(dve.tensor_tensor(brow[0:TT, :], acc[0:TT, 7, 0:NT], dis[0:TT, :], ALU.mult))
            for m in range(KC):
                dve.wait_ge(z_hi, m + 1)
                dve.tensor_tensor(halves(b_lo[:, m, :]), acc_dense(m % 2), halves(b_hi[:, m, :].bitcast(f32)),
                                  ALU.subtract).then_inc(z_lo, 1)
                if m == 2:
                    dve.wait_ge(x_again, 16)
                    dve.wait_ge(gnn_b_loaded, 16)
                if 2 <= m < 2 + NT:
                    r = rows[0:TT, m - 2, :]
                    last = dve.scalar_tensor_tensor(out=r, in0=gnn_bb[0:TT, :], scalar=brow[0:TT, m - 2:m - 1],
                                                    in1=r, op0=ALU.mult, op1=ALU.add)
                    if m == 1 + NT:
                        link(last)
            dve.wait_ge(z_done, KC)
            dve.memset(a_hi[:, :, T:TP].bitcast(f32), 0.0).then_inc(pads_zero, 1)
            dve.memset(a_lo[:, :, T:TP].bitcast(f32), 0.0).then_inc(pads_zero, 1)

            def tp_tokens(pair, i):
                b = TPB + 2 * pair + (i == 4)
                return acc[0:TT, b, (i % 4) * P:(i % 4) * P + P]

            last_stat = [None]

            def block_stats(m):
                dve.wait_ge(gnn_x1, m + 1)
                for i in range(NT):
                    last_stat[0] = dve.bn_stats(stats[0:TT, i, m, :], rows[0:TT, i, m * P:(m + 1) * P])

            for m in range(KC):
                dve.wait_ge(gnn_tp, m + 1)
                for i in range(NT):
                    r = rows[0:TT, i, m * P:(m + 1) * P]
                    last = dve.scalar_tensor_tensor(out=r, in0=tp_tokens(m % 2, i), scalar=dis[0:TT, i:i + 1],
                                                    in1=r, op0=ALU.mult, op1=ALU.add)
                last.then_inc(gnn_x1, 1)
                if m >= 1:
                    block_stats(m - 1)
            block_stats(KC - 1)
            link(last_stat[0])
            for i in range(NT):
                a = dve.bn_aggr(mv[0:TT, i, :], stats[0:TT, i, :, :].rearrange("p h s -> p (h s)"))
            link(a)
            dve.tensor_scalar(mv[0:TT, :, 1], mv[0:TT, :, 1], 1e-5, None, ALU.add).then_inc(ln_var, 1)
            dve.wait_ge(ln_root, 1)
            link(dve.reciprocal(rstd[0:TT, :], rstd[0:TT, :]))

            def ln_low(i):
                for q in range(2):
                    dve.wait_ge(ln_hi, 2 * i + q + 1)
                    o = slice(4 * q, 4 * q + 4), slice(i * TT, (i + 1) * TT)
                    dve.tensor_tensor(a_lo[:, o[0], o[1]],
                                      acc[:, TPB + (2 * i + q) % 4, 0:4 * TT].rearrange("p (k t) -> p k t", k=4),
                                      a_hi[:, o[0], o[1]].bitcast(f32), ALU.subtract).then_inc(ln_lo, 1)

            for i in range(NT):
                if i >= 3:
                    dve.wait_ge(ln_tp, 2 * (i - 2))
                dve.tensor_scalar(grow[0:TT, i % 3, :], rows[0:TT, i, :], mv[0:TT, i, 0:1], rstd[0:TT, i:i + 1],
                                  ALU.subtract, ALU.mult).then_inc(ln_rows, 1)
                if i >= 1:
                    ln_low(i - 1)
            ln_low(NT - 1)

            def linear_lo(st, o_hi, o_lo, b):
                for m in range(KC):
                    dve.wait_ge(st.hi, m + 1)
                    dve.scalar_tensor_tensor(out=halves(o_lo[:, m, :]), in0=acc_dense(m % 2),
                                             scalar=bias[:, b, m:m + 1], in1=halves(o_hi[:, m, :].bitcast(f32)),
                                             op0=ALU.add, op1=ALU.subtract).then_inc(st.lo, 1)

            def gated_pair(st, m, o_hi, o_lo, b, tp=None):
                dve.wait_ge(unit_done, st.base + 2 * m + 2)
                dve.wait_ge(st.silu, m + 1)
                if tp is not None and m >= 2:
                    dve.wait_ge(tp, m - 1)
                if b is None:
                    dve.tensor_tensor(halves(prod[:, m % 2, :]), acc_dense(1), halves(silu[:, :]),
                                      ALU.mult).then_inc(st.prod, 1)
                else:
                    dve.scalar_tensor_tensor(out=halves(prod[:, m % 2, :]), in0=acc_dense(1),
                                             scalar=bias[:, b, m:m + 1], in1=halves(silu[:, :]),
                                             op0=ALU.add, op1=ALU.mult).then_inc(st.prod, 1)
                if o_lo is not None:
                    dve.wait_ge(st.hi, m + 1)
                    dve.tensor_tensor(o_lo[:, m, :], prod[:, m % 2, :], o_hi[:, m, :].bitcast(f32),
                                      ALU.subtract).then_inc(st.lo, 1)

            linear_lo(lin0, b_hi, b_lo, B_LIN0)
            dve.wait_ge(gate_split, 1)
            dve.tensor_tensor(gate_lo, gate_raw, gate_hi.bitcast(f32), ALU.subtract).then_inc(gate_split, 1)

            def h_rows(m):
                dve.wait_ge(h_tp, m + 1)
                if m == 0:
                    dve.wait_ge(x1_saved, 16)
                dve.tensor_copy(rows[0:TT, 0:4, m * P:(m + 1) * P],
                                acc[0:TT, TPB + 2 * (m % 2), :].rearrange("p (i d) -> p i d", d=P))
                dve.tensor_copy(rows[0:TT, 4, m * P:(m + 1) * P], tp_tokens(m % 2, 4)).then_inc(h_copied, 1)

            for m in range(KC):
                gated_pair(swi1, m, a_hi, a_lo, B_S1B, h_tp)
                if m >= 1:
                    h_rows(m - 1)
            h_rows(KC - 1)

            def bc(ap, axis):
                return ap.unsqueeze(axis)

            def route_scores():
                dve.wait_ge(logits_done, 1)
                lo = acc[0:TT, TPB + 2, 0:NT * EXPERTS].rearrange("p (i e) -> p i e", e=EXPERTS)
                link(dve.tensor_reduce(col1[0:TT, :], lo, AX.X, ALU.max))
                dve.tensor_tensor(lg[0:TT, :, :], lo, col1[0:TT, :].unsqueeze(2).to_broadcast([TT, NT, EXPERTS]),
                                  ALU.subtract).then_inc(shifted, 1)
                dve.wait_ge(exped, 1)
                link(dve.tensor_reduce(col1[0:TT, :], score[0:TT, :, :], AX.X, ALU.add))
                link(dve.reciprocal(col1[0:TT, :], col1[0:TT, :]))
                link(dve.tensor_tensor(score[0:TT, :, :], score[0:TT, :, :],
                                       col1[0:TT, :].unsqueeze(2).to_broadcast([TT, NT, EXPERTS]), ALU.mult))
                sj = score[0:TT, :, :].unsqueeze(2).to_broadcast([TT, NT, EXPERTS, EXPERTS])
                se = score[0:TT, :, :].unsqueeze(3).to_broadcast([TT, NT, EXPERTS, EXPERTS])
                dve.wait_ge(tri_set, 5)
                dve.tensor_tensor(cmp_gt[0:TT], sj, se, ALU.is_gt)
                link(dve.tensor_tensor(cmp_eq[0:TT], sj, se, ALU.is_equal))
                link(dve.tensor_tensor(cmp_eq[0:TT], cmp_eq[0:TT],
                                       lower[0:TT].unsqueeze(1).to_broadcast([TT, NT, EXPERTS, EXPERTS]), ALU.mult))
                link(dve.tensor_tensor(cmp_gt[0:TT], cmp_gt[0:TT], cmp_eq[0:TT], ALU.add))
                link(dve.tensor_reduce(rank[0:TT, :, :], cmp_gt[0:TT], AX.X, ALU.add))
                dve.tensor_scalar(mask[0:TT, :, :], rank[0:TT, :, :], float(TOP), None, ALU.is_lt)
                dve.tensor_scalar(mask16[0:TT, :, :], rank[0:TT, :, :], float(TOP), None,
                                  ALU.is_lt).then_inc(mask_ready, 1)

            def picks(rows_of, weights_of, to_rows, to_weights):
                for k in range(TOP):
                    for what, to in ((rows_of, to_rows), (weights_of, to_weights)):
                        link(dve.scalar_tensor_tensor(out=pick[0:TT, :, :], in0=rank[0:TT, :, :], scalar=float(k),
                                                      in1=what[0:TT, :, :], op0=ALU.is_equal, op1=ALU.mult))
                        link(dve.tensor_reduce(to[0:TT, k, :], pick[0:TT, :, :], AX.X, ALU.add))

            def route_slots():
                dve.wait_ge(slots_done, 1)
                pos = acc[0:TT, TPB + 1, 0:NT * EXPERTS].rearrange("p (i e) -> p i e", e=EXPERTS)
                tot = acc[0:TT, TPB + 1, NT * EXPERTS:(NT + 1) * EXPERTS]
                link(dve.tensor_reduce(most[0:TT, :], tot, AX.X, ALU.max))
                link(dve.tensor_copy(most_i[0:TT, :], most[0:TT, :]))
                dve.tensor_copy(used_i[0:TT, :], tot)
                link(dve.scalar_tensor_tensor(out=slot[0:TT, :, :], in0=pos, scalar=1.0, in1=mask[0:TT, :, :],
                                              op0=ALU.add, op1=ALU.mult))
                link(dve.tensor_scalar(slot[0:TT, :, :], slot[0:TT, :, :], -1.0, None, ALU.add))
                link(dve.tensor_tensor(score[0:TT, :, :], score[0:TT, :, :], mask[0:TT, :, :], ALU.mult))
                link(dve.tensor_reduce(col1[0:TT, :], score[0:TT, :, :], AX.X, ALU.add))
                link(dve.reciprocal(col1[0:TT, :], col1[0:TT, :]))
                link(dve.tensor_tensor(score[0:TT, :, :], score[0:TT, :, :],
                                       col1[0:TT, :].unsqueeze(2).to_broadcast([TT, NT, EXPERTS]), ALU.mult))
                link(dve.scalar_tensor_tensor(out=lg[0:TT, :, :], in0=pos, scalar=float(CAP), in1=score[0:TT, :, :],
                                              op0=ALU.is_lt, op1=ALU.mult))
                for e in range(EXPERTS):
                    last = dve.tensor_scalar(ykey[0:TT, :, e], pos[:, :, e], float(CAP - 1), float(e * CAP),
                                             ALU.min, ALU.add)
                link(last)
                picks(ykey, lg, top_row, top_w)
                dve.tensor_copy(top_idx[0:TT, :, :], top_row[0:TT, :, :]).then_inc(routed, 1)

            def slot_onehots(q):
                if q >= 1:
                    dve.wait_ge(tok_done, q)
                for e in range(2):
                    for i in range(NT):
                        last = dve.tensor_scalar(onehot[0:TT, e, i, :], iota[0:TT, 0:CAP],
                                                 slot[0:TT, i, 2 * q + e:2 * q + e + 1], None, ALU.is_equal)
                last.then_inc(oh_ready, 1)

            def token_lists(q):
                dve.wait_ge(tok_done, q + 1)
                for e in range(2):
                    t = acc[:, TPB + 2, 4 * e:4 * e + 3]
                    c = 3 * (2 * q + e)
                    dve.tensor_copy(slot_tok[:, c:c + 2], t[:, 0:2])
                    last = dve.tensor_copy(slot_tok[0:CAP - 2 * P, c + 2:c + 3], t[0:CAP - 2 * P, 2:3])
                last.then_inc(tok_copied, 1)

            for m in range(KC):
                gated_pair(sha, m, b_hi, b_lo, None)
                if m == 0:
                    dve.wait_ge(logits_summed, 1)
                    dve.tensor_copy(halves(logits_t), acc[0:EXPERTS, TPB:TPB + 2, 0:HT]).then_inc(logits_copied, 1)
                if m == 1:
                    route_scores()
                if m == 2:
                    route_slots()
                    slot_onehots(0)
                if 3 <= m <= 6:
                    token_lists(m - 3)
                    if m < 6:
                        slot_onehots(m - 2)

            def expert_in_lo(e, m):
                dve.wait_ge(xe_hi, e * KC + (m + 1))
                dve.tensor_tensor(e_lo[:, m, :], acc[:, TPB + 2 + m % 2, 0:CAP], e_hi[:, m, :].bitcast(f32),
                                  ALU.subtract).then_inc(xe_lo, 1)

            for m in range(KC):
                expert_in_lo(0, m)

            def y_rows(e, m):
                dve.wait_ge(y_tp, e * KC + (m + 1))
                b = acc[:, TPB + m % 2, :]
                cn = CAP - 2 * P
                dve.tensor_copy(yrow[:, 0:2, m * P:(m + 1) * P], b[:, 0:2 * P].rearrange("p (s d) -> p s d", d=P))
                dve.tensor_copy(yrow[0:cn, 2, m * P:(m + 1) * P], b[0:cn, 2 * P:3 * P]).then_inc(y_copied, 1)

            def expert(e, nxt, prev=True):
                base = e * UNITS_EXPERT + U_EXP
                for m in range(KC):
                    dve.wait_ge(unit_done, base + (2 * m + 2))
                    dve.wait_ge(exp.silu, e * KC + (m + 1))
                    dve.tensor_tensor(prod[:, m % 2, 0:CAP], acc[:, (2 * m + 1) % 4, 0:CAP], silu[:, 0:CAP],
                                      ALU.mult).then_inc(exp.prod, 1)
                    dve.wait_ge(exp.hi, e * KC + (m + 1))
                    dve.tensor_tensor(g_lo[:, m, :], prod[:, m % 2, 0:CAP], g_hi[:, m, :].bitcast(f32),
                                      ALU.subtract).then_inc(exp.lo, 1)
                if prev:
                    dve.wait_ge(y_saved, e * (16 * 3))
                for m in range(KC):
                    if m >= 1:
                        y_rows(e, m - 1)
                    if nxt:
                        expert_in_lo(e + 1, m)
                y_rows(e, KC - 1)

            expert(0, True, prev=False)
            with dve.Fori(1, EXPERTS - 1) as e:
                expert(e, True)
            expert(EXPERTS - 1, False)

            def add_back(i):
                for k in range(TOP):
                    dve.wait_ge(back[k], 16 * (i + 1))
                    w = top_w[0:TT, k, i:i + 1]
                    if k == 0:
                        if i >= 2:
                            dve.wait_ge(sum_tp, 2 * (i - 1))
                        dve.tensor_scalar(sum_slot(i), back_slot(k), w, None, ALU.mult).then_inc(back_used, 1)
                    else:
                        dve.wait_ge(back_used, TOP * i + k)
                        dve.scalar_tensor_tensor(out=sum_slot(i), in0=back_slot(k), scalar=w,
                                                 in1=sum_slot(i), op0=ALU.mult,
                                                 op1=ALU.add).then_inc(back_used, 1)

            ys = rows[:, :, :].rearrange("p i d -> p (i d)")[:, 0:KC * TP].rearrange("p (k t) -> p k t", t=TP)

            def add_tile(i):
                for q in range(2):
                    dve.wait_ge(sum_tp, 2 * i + q + 1)
                    add_to_sum(TPB + q, i, q, sum_used)

            def add_to_sum(bank, i, q, done):
                y = ys[:, 4 * q:4 * q + 4, i * TT:(i + 1) * TT]
                return dve.tensor_tensor(y, y, acc[:, bank, 0:4 * TT].rearrange("p (k t) -> p k t", t=TT),
                                         ALU.add).then_inc(done, 1)

            with dve.If(fullest(dve) > CAP):
                main_chain = chain[:]
                chain[:] = [ov_chain, 0]
                dve.wait_ge(ov_ready, 1)
                with dve.Fori(0, OV_ROUNDS) as c:
                    with dve.Fori(0, EXPERTS) as e:
                        n = c * EXPERTS + e

                        def low_part(count):
                            dve.wait_ge(ov_hi, count + 1)
                            dve.tensor_tensor(w_lo[:, OVS, :], ov_raw, w_hi[:, OVS, :].bitcast(f32),
                                              ALU.subtract).then_inc(ov_lo, 1)

                        for i in range(NT):
                            last = dve.tensor_scalar(ov_onehot[0:TT, i, :],
                                                     ov_iota[0:TT, bass.ds(c * OV_SLOTS, OV_SLOTS)],
                                                     slot[0:TT, i, bass.ds(e, 1)], None, ALU.is_equal)
                        last.then_inc(ov_oh, 1)
                        dve.wait_ge(ov_tok, n + 1)
                        dve.tensor_copy(now_tok[:, 0:1], acc[:, TPB, 0:1]).then_inc(ov_tok_copied, 1)
                        for q in range(2):
                            dve.wait_ge(ov_xhi, n * 2 + (q + 1))
                            dve.tensor_tensor(e_lo[:, 4 * q:4 * q + 4, 0:OV_SLOTS],
                                              acc[:, TPB + 1 + q, :].rearrange("p (k t) -> p k t", k=4),
                                              e_hi[:, 4 * q:4 * q + 4, 0:OV_SLOTS].bitcast(f32),
                                              ALU.subtract).then_inc(ov_xlo, 1)
                        with dve.Fori(0, KC) as m:
                            low_part(n * UNITS_EXPERT + m * 2)
                            low_part(n * UNITS_EXPERT + m * 2 + 1)
                            dve.wait_ge(ov_unit, n * UNITS_EXPERT + m * 2 + 2)
                            dve.wait_ge(ov_silu, n * KC + m + 1)
                            dve.tensor_tensor(prod[:, 0, 0:OV_SLOTS], acc[:, 1, 0:OV_SLOTS], silu[:, 0:OV_SLOTS],
                                              ALU.mult).then_inc(ov_prod, 1)
                            dve.wait_ge(ov_ghi, n * KC + m + 1)
                            at = [t[:, bass.ds(m, 1), 0:OV_SLOTS].rearrange("p m t -> p (m t)")
                                  for t in (g_lo, g_hi)]
                            dve.tensor_tensor(at[0], prod[:, 0, 0:OV_SLOTS], at[1].bitcast(f32),
                                              ALU.subtract).then_inc(ov_glo, 1)
                        with dve.Fori(0, KC) as m:
                            low_part(n * UNITS_EXPERT + m + UNITS_UP)
                            dve.wait_ge(ov_yx, n * KC + m + 1)
                            dve.tensor_copy(ov_out[:, bass.ds(m * P, P)], acc[:, TPB + 3, 0:P]).then_inc(ov_y, 1)
                for e in range(EXPERTS):
                    last = dve.tensor_scalar(ykey[0:TT, :, e], slot[0:TT, :, e], float(-CAP), 0.0, ALU.add, ALU.max)
                link(last)
                for e in range(EXPERTS):
                    last = dve.tensor_scalar(ykey[0:TT, :, e], ykey[0:TT, :, e], float(e * OV_ALL), None, ALU.add)
                link(last)
                link(dve.scalar_tensor_tensor(out=lg[0:TT, :, :], in0=slot[0:TT, :, :], scalar=float(CAP),
                                              in1=score[0:TT, :, :], op0=ALU.is_ge, op1=ALU.mult))
                picks(ykey, lg, top_row, ov_w)
                dve.tensor_copy(ov_idx[0:TT, :, :], top_row[0:TT, :, :]).then_inc(ov_routed, 1)
                for n in range(NT * TOP):
                    i, k = divmod(n, TOP)
                    dve.wait_ge(ov_back, 16 * (n + 1))
                    w = ov_w[0:TT, k, i:i + 1]
                    if k == 0:
                        dve.tensor_scalar(ov_out[0:TT, :], ov_in[0:TT, :], w, None, ALU.mult).then_inc(ov_used, 1)
                    else:
                        dve.wait_ge(ov_used, n)
                        dve.scalar_tensor_tensor(out=ov_out[0:TT, :], in0=ov_in[0:TT, :], scalar=w,
                                                 in1=ov_out[0:TT, :], op0=ALU.mult, op1=ALU.add).then_inc(ov_used, 1)
                    if k == TOP - 1:
                        for q in range(2):
                            dve.wait_ge(ov_sum, 2 * i + q + 1)
                            add_to_sum(TPB + 1 + q, i, q, ov_added)
                dve.wait_ge(ov_added, 2 * NT)
                chain[:] = main_chain

            for m in range(KC):
                gated_pair(shb, m, b_hi, b_lo, None)
                if 2 <= m < NT + 2:
                    add_tile(m - 2)
                if 1 <= m <= NT:
                    add_back(m - 1)
            for m in range(KC):
                dve.wait_ge(unit_done, U_SHB + UNITS_UP + m + 1)
                if m == 0:
                    dve.wait_ge(sum_used, 2 * NT)
                dve.tensor_tensor(halves(prod[:, m % 2, :]), acc_dense(m % 2), halves(ysum(m)),
                                  ALU.add).then_inc(shb_sum, 1)
                dve.wait_ge(shb_dhi, m + 1)
                dve.tensor_tensor(a_lo[:, m, :], prod[:, m % 2, :], a_hi[:, m, :].bitcast(f32),
                                  ALU.subtract).then_inc(shb_dlo, 1)
            linear_lo(lin1, b_hi, b_lo, B_LIN1)

            def out_rows(m):
                dve.wait_ge(o_tp, m + 1)
                if m == 0:
                    dve.wait_ge(x1_back, 16)
                r = rows[0:TT, 0:4, m * P:(m + 1) * P]
                dve.tensor_tensor(r, acc[0:TT, TPB + 2 * (m % 2), :].rearrange("p (i d) -> p i d", d=P), r, ALU.add)
                r = rows[0:TT, 4, m * P:(m + 1) * P]
                dve.tensor_tensor(r, tp_tokens(m % 2, 4), r, ALU.add).then_inc(o_rows, 1)

            for m in range(KC):
                gated_pair(swi2, m, None, None, B_S2B, o_tp)
                if m >= 1:
                    out_rows(m - 1)
            out_rows(KC - 1)

        @block.tensor
        def _(pe):
            pe.wait_ge(const_ready, 6)
            n0 = 0
            for g, chunks in enumerate(GROUPS):
                outs = [acc[0:TT, count_bank(g, i), 0:HT] for i in range(NT)]
                for i in range(NT):
                    if NT * g + i >= 8:
                        pe.wait_ge(banks_read, NT * g + i - 7)
                    pe.matmul(outs[i], zeros[0:TT, 0:TT], zeros[0:TT, 0:HT], start=True, stop=False)
                with pe.Fori(n0 // OHR, (n0 + chunks) // OHR) as it:
                    for s in range(OHR):
                        pe.wait_ge(onehot_ready, it * OHR + (s + 1))
                        for i in range(NT):
                            last = pe.matmul(outs[i], oh_dst[0:TT, s, i * TT:(i + 1) * TT],
                                             oh_src[0:TT, s, :], start=False, stop=False)
                        last.then_inc(onehot_used, 1)
                for i in range(NT):
                    last = pe.matmul(outs[i], zeros[0:TT, 0:TT], zeros[0:TT, 0:HT], start=False, stop=True)
                last.then_inc(counts_done, 1)
                n0 += chunks

            def column_sums(bank, rhs, done):
                for r in range(NT):
                    for i in range(NT):
                        last = pe.matmul(acc[0:TT, bank, r:r + 1], counts[0:TT, i, r * TT:(r + 1) * TT], rhs(i),
                                         start=(i == 0), stop=(i == NT - 1))
                last.then_inc(done, 1)

            pe.wait_ge(counts_read, NT)
            column_sums(0, lambda i: ones[0:TT, 0:1], deg_done)
            pe.wait_ge(dis_ready, 1)
            column_sums(7, lambda i: dis[0:TT, i:i + 1], sums_done)

            def products(outs, hi, lo, x_hi, x_lo, first, last):
                for w, xs_ in ((hi, x_hi), (hi, x_lo), (lo, x_hi)):
                    for h, o in enumerate(outs):
                        ins = pe.matmul(o, w, xs_[h], start=(first and w is hi and xs_ is x_hi),
                                        stop=(last and w is lo))
                return ins

            for m in range(KC):
                if m >= 2:
                    pe.wait_ge(z_lo, m - 1)
                outs = [acc[:, 2 * (m % 2) + h, 0:HT] for h in range(2)]
                for i in range(NT):
                    if m == 0:
                        pe.wait_ge(counts_lo, i + 1)
                        pe.wait_ge(xs_lo_ready, i + 1)
                    c = [[cc[0:TT, i, h * HT:(h + 1) * HT] for h in range(2)] for cc in (c_hi, c_lo)]
                    last = products(outs, xs_hi[0:TT, i, m * P:(m + 1) * P], xs_lo[0:TT, i, m * P:(m + 1) * P],
                                    c[0], c[1], i == 0, i == NT - 1)
                last.then_inc(z_done, 1)

            def unit(u, off, x_hi, x_lo, banks, width, ready=None):
                s = off % RING
                if isinstance(u, int):
                    pe.wait_ge(hi_split, u + off + 1)
                    pe.wait_ge(lo_split, u + off + 1)
                else:
                    pe.wait_ge(hi_split, u + (off + 1))
                    pe.wait_ge(lo_split, u + (off + 1))
                outs = [acc[:, b, 0:width] for b in banks]
                for k in range(KC):
                    if ready is not None:
                        ready(k)
                    xx = [[t[:, k, h * width:(h + 1) * width] for h in range(len(banks))] for t in (x_hi, x_lo)]
                    last = products(outs, w_hi[:, s, k * P:(k + 1) * P], w_lo[:, s, k * P:(k + 1) * P],
                                    xx[0], xx[1], k == 0, k == KC - 1)
                last.then_inc(unit_done, 1)

            def dense(u, off, x_hi, x_lo, ready=None):
                unit(u, off, x_hi, x_lo, (2 * (off % 2), 2 * (off % 2) + 1), HT, ready)

            def both(hi, lo):
                def ready(k):
                    pe.wait_ge(hi, k + 1)
                    pe.wait_ge(lo, k + 1)
                return ready

            def to_rows(src_t, pair, done):
                for i in range(NT):
                    b = TPB + 2 * pair + (i == 4)
                    last = pe.transpose(acc[0:TT, b, (i % 4) * P:(i % 4) * P + P],
                                        src_t[:, i * TT:(i + 1) * TT], ident[:, :])
                last.then_inc(done, 1)

            def gnn_turn(m):
                pe.wait_ge(gnn_copy, m + 1)
                if m >= 2:
                    pe.wait_ge(gnn_x1, m - 1)
                to_rows(prod[:, m % 2, :], m % 2, gnn_tp)

            for m in range(KC):
                if m >= 2:
                    pe.wait_ge(gnn_copy, m - 1)
                elif m == 0:
                    pe.wait_ge(z_lo, KC - 1)
                dense(U_GNN, m, b_hi, b_lo, both(z_hi, z_lo) if m == 0 else None)
                if m == 0:
                    pe.wait_ge(z_lo, KC)
                if m >= 1:
                    gnn_turn(m - 1)
            gnn_turn(KC - 1)

            for i in range(NT):
                pe.wait_ge(ln_rows, i + 1)
                for q in range(2):
                    n = 2 * i + q
                    if n >= 4:
                        pe.wait_ge(ln_lo, n - 3)
                    elif n == 0:
                        pe.wait_ge(gnn_x1, KC)
                    for k in range(4):
                        last = pe.transpose(acc[:, TPB + n % 4, k * TT:(k + 1) * TT],
                                            grow[0:TT, i % 3, (4 * q + k) * P:(4 * q + k + 1) * P],
                                            ident[0:TT, 0:TT])
                    last.then_inc(ln_tp, 1)

            def linear(st, x_hi, x_lo, first_ready, freed):
                for m in range(KC):
                    if m >= 2:
                        pe.wait_ge(st.lo, m - 1)
                    elif m == 0:
                        freed()
                    dense(st.base, m, x_hi, x_lo, first_ready if m == 0 else None)

            def gated(st, x_hi, x_lo, first_ready, after=None, freed=None):
                for m in range(KC):
                    if m >= 1:
                        pe.wait_ge(st.silu, m)
                    elif freed is not None:
                        freed()
                    dense(st.base, 2 * m, x_hi, x_lo, first_ready if m == 0 else None)
                    if m >= 1:
                        pe.wait_ge(st.prod, m)
                    dense(st.base, 2 * m + 1, x_hi, x_lo)
                    if after is not None:
                        after(m)

            pe.wait_ge(ln_hi, 2 * NT)
            pe.wait_ge(ln_lo, 2 * NT)
            pe.wait_ge(pads_zero, 2)
            linear(lin0, a_hi, a_lo, None, lambda: pe.wait_ge(gnn_copy, KC))

            def h_turn(m):
                pe.wait_ge(swi1.prod, m + 1)
                if m >= 2:
                    pe.wait_ge(h_copied, m - 1)
                to_rows(prod[:, m % 2, :], m % 2, h_tp)

            gated(swi1, b_hi, b_lo, both(lin0.hi, lin0.lo), lambda m: h_turn(m - 1) if m >= 1 else None,
                  lambda: pe.wait_ge(lin0.lo, KC - 1))
            h_turn(KC - 1)

            def sha_extra(m):
                if m == 0:
                    pe.wait_ge(gate_split, 2)
                    pe.wait_ge(h_copied, KC)
                    outs = [acc[:, TPB + h, 0:HT] for h in range(2)]
                    for k in range(KC):
                        xx = [[t[:, k, h * HT:(h + 1) * HT] for h in range(2)] for t in (a_hi, a_lo)]
                        last = products(outs, gate_hi[:, k * P:(k + 1) * P], gate_lo[:, k * P:(k + 1) * P],
                                        xx[0], xx[1], k == 0, k == KC - 1)
                    last.then_inc(logits_summed, 1)
                if m == 1:
                    pe.wait_ge(logits_copied, 1)
                    for i in range(NT):
                        last = pe.transpose(acc[0:TT, TPB + 2, i * EXPERTS:(i + 1) * EXPERTS],
                                            logits_t[:, i * TT:(i + 1) * TT], ident[0:EXPERTS, 0:EXPERTS])
                    last.then_inc(logits_done, 1)
                if m == 2:
                    pe.wait_ge(mask_ready, 1)
                    for i in range(NT + 1):
                        o = acc[0:TT, TPB + 1, i * EXPERTS:(i + 1) * EXPERTS]
                        for j in range(min(i, NT - 1) + 1):
                            w = tri[0:TT, :] if j == i else full16[0:TT, 0:TT]
                            last = pe.matmul(o, w, mask16[0:TT, j, :], start=(j == 0), stop=(j == min(i, NT - 1)))
                    last.then_inc(slots_done, 1)
                if 3 <= m <= 6:
                    q = m - 3
                    pe.wait_ge(oh_ready, q + 1)
                    if q >= 1:
                        pe.wait_ge(tok_copied, q)
                    for e in range(2):
                        for n, (c0, cn) in enumerate(SLOT_TILES):
                            for i in range(NT):
                                last = pe.matmul(acc[0:cn, TPB + 2, 4 * e + n:4 * e + n + 1],
                                                 onehot[0:TT, e, i, c0:c0 + cn], tok_id[0:TT, i:i + 1],
                                                 start=(i == 0), stop=(i == NT - 1))
                    last.then_inc(tok_done, 1)

            gated(sha, a_hi, a_lo, both(swi1.hi, swi1.lo), sha_extra)

            def expert_in(e, m):
                if isinstance(e, int):
                    if m == 0:
                        pe.wait_ge(gathered, 16 * 3 * (e + 1))
                else:
                    if m == 0:
                        pe.wait_ge(gathered, e * (16 * 3) + 16 * 3)
                if m >= 2:
                    pe.wait_ge(xe_lo, e * KC + (m - 1))
                for n, (c0, cn) in enumerate(SLOT_TILES):
                    last = pe.transpose(acc[:, TPB + 2 + m % 2, c0:c0 + cn], grow[0:cn, n, m * P:(m + 1) * P],
                                        ident[0:cn, 0:cn])
                last.then_inc(xe_tp, 1)

            for m in range(KC):
                if m >= 2:
                    pe.wait_ge(sha_y, m - 1)
                elif m == 0:
                    pe.wait_ge(sha.silu, KC)
                else:
                    pe.wait_ge(sha.prod, KC)
                dense(U_SHA + UNITS_UP, m, b_hi, b_lo, both(sha.hi, sha.lo) if m == 0 else None)
                if m == 0:
                    pe.wait_ge(tok_copied, 4)
                expert_in(0, m)

            def turn_y(e, m):
                pe.wait_ge(yt_copied, e * KC + (m + 1))
                if m >= 2:
                    pe.wait_ge(y_copied, e * KC + (m - 1))
                for n, (c0, cn) in enumerate(SLOT_TILES):
                    last = pe.transpose(acc[0:cn, TPB + m % 2, n * P:(n + 1) * P], prod[:, m % 2, c0:c0 + cn],
                                        ident[:, :])
                last.then_inc(y_tp, 1)

            def expert(e, nxt, width):
                base = e * UNITS_EXPERT + U_EXP

                def in_ready(k):
                    pe.wait_ge(xe_hi, e * KC + (k + 1))
                    pe.wait_ge(xe_lo, e * KC + (k + 1))

                def hidden_ready(k):
                    pe.wait_ge(exp.hi, e * KC + (k + 1))
                    pe.wait_ge(exp.lo, e * KC + (k + 1))

                for j in range(UNITS_UP):
                    m = j // 2
                    if m >= 2:
                        pe.wait_ge(exp.silu if j % 2 == 0 else exp.prod, e * KC + (m - 1))
                    unit(base, j, e_hi, e_lo, (j % 4,), width, in_ready if j == 0 else None)
                for m in range(KC):
                    if m >= 4:
                        pe.wait_ge(yt_copied, e * KC + (m - 3))
                    elif m == 0:
                        pe.wait_ge(exp.silu, e * KC + KC)
                    elif m == 1:
                        pe.wait_ge(exp.prod, e * KC + KC)
                    unit(base, UNITS_UP + m, g_hi, g_lo, (m % 4,), width, hidden_ready if m == 0 else None)
                    if m >= 1:
                        turn_y(e, m - 1)
                    if nxt:
                        expert_in(e + 1, m)
                turn_y(e, KC - 1)

            def expert_of(e, nxt):
                tokens = pe.value_load(used_i[0:1, bass.ds(e, 1)], min_val=0, max_val=T)

                def choose(widths):
                    if len(widths) == 1:
                        expert(e, nxt, widths[0])
                    else:
                        with pe.If(tokens <= widths[0]):
                            expert(e, nxt, widths[0])
                        with pe.Else():
                            choose(widths[1:])

                choose(WIDTHS)

            pe.wait_ge(sha_y, KC)
            for b in range(4):
                pe.matmul(acc[:, b, 0:CAP], full16[0:TT, :], onehot[0:TT, 0, 0, :], start=True, stop=True)
            pe.wait_ge(routed, 1)
            with pe.Fori(0, EXPERTS - 1) as e:
                expert_of(e, True)
            expert_of(EXPERTS - 1, False)

            def shb_extra(m):
                if 2 <= m < NT + 2:
                    i = m - 2
                    pe.wait_ge(back_used, TOP * (i + 1))
                    for q in range(2):
                        if i >= 1:
                            pe.wait_ge(sum_used, 2 * (i - 1) + q + 1)
                        elif q == 0:
                            pe.wait_ge(y_copied, EXPERTS * KC)
                        for k in range(4):
                            last = pe.transpose(acc[:, TPB + q, k * TT:(k + 1) * TT],
                                                sum_slot(i)[:, (4 * q + k) * P:(4 * q + k + 1) * P],
                                                ident[0:TT, 0:TT])
                        last.then_inc(sum_tp, 1)

            with pe.If(fullest(pe) > CAP):
                pe.wait_ge(y_copied, EXPERTS * KC)
                pe.wait_ge(yt_copied, EXPERTS * KC)

                def ov_products(count, bank, x_hi, x_lo):
                    pe.wait_ge(ov_lo, count + 1)
                    for k in range(KC):
                        last = products([acc[:, bank, 0:OV_SLOTS]], w_hi[:, OVS, k * P:(k + 1) * P],
                                        w_lo[:, OVS, k * P:(k + 1) * P], [x_hi[:, k, 0:OV_SLOTS]],
                                        [x_lo[:, k, 0:OV_SLOTS]], k == 0, k == KC - 1)
                    last.then_inc(ov_unit, 1)

                with pe.Fori(0, OV_ROUNDS) as c:
                    with pe.Fori(0, EXPERTS) as e:
                        n = c * EXPERTS + e
                        pe.wait_ge(ov_oh, n + 1)
                        for i in range(NT):
                            last = pe.matmul(acc[:, TPB, 0:1], ov_onehot[0:TT, i, :], tok_id[0:TT, i:i + 1],
                                             start=(i == 0), stop=(i == NT - 1))
                        last.then_inc(ov_tok, 1)
                        pe.wait_ge(ov_gathered, n * 16 + 16)
                        for k in range(KC):
                            last = pe.transpose(acc[:, TPB + 1 + k // 4, (k % 4) * P:(k % 4) * P + P],
                                                ov_in[:, k * P:(k + 1) * P], ident[:, :])
                        last.then_inc(ov_xt, 1)
                        with pe.Fori(0, KC) as m:
                            pe.wait_ge(ov_xlo, n * 2 + 2)
                            ov_products(n * UNITS_EXPERT + m * 2, 0, e_hi, e_lo)
                            ov_products(n * UNITS_EXPERT + m * 2 + 1, 1, e_hi, e_lo)
                        with pe.Fori(0, KC) as m:
                            pe.wait_ge(ov_glo, n * KC + KC)
                            ov_products(n * UNITS_EXPERT + m + UNITS_UP, 0, g_hi, g_lo)
                            pe.wait_ge(ov_yt, n * KC + m + 1)
                            pe.transpose(acc[:, TPB + 3, 0:P], prod[:, 1, 0:OV_SLOTS], ident[:, :]).then_inc(ov_yx, 1)
                for i in range(NT):
                    pe.wait_ge(ov_used, TOP * (i + 1))
                    for q in range(2):
                        if i >= 1:
                            pe.wait_ge(ov_added, 2 * (i - 1) + q + 1)
                        for k in range(4):
                            last = pe.transpose(acc[:, TPB + 1 + q, k * TT:(k + 1) * TT],
                                                ov_out[0:TT, (4 * q + k) * P:(4 * q + k + 1) * P],
                                                ident[0:TT, 0:TT])
                        last.then_inc(ov_sum, 1)
                pe.wait_ge(ov_added, 2 * NT)

            pe.wait_ge(yt_copied, EXPERTS * KC)
            gated(shb, a_hi, a_lo, None, shb_extra)
            for m in range(KC):
                if m >= 2:
                    pe.wait_ge(shb_sum, m - 1)
                elif m == 0:
                    pe.wait_ge(shb.silu, KC)
                else:
                    pe.wait_ge(shb.prod, KC)
                dense(U_SHB + UNITS_UP, m, b_hi, b_lo, both(shb.hi, shb.lo) if m == 0 else None)
            linear(lin1, a_hi, a_lo, both(shb_dhi, shb_dlo), lambda: pe.wait_ge(shb_sum, KC - 1))

            def o_turn(m):
                pe.wait_ge(swi2.prod, m + 1)
                if m >= 2:
                    pe.wait_ge(o_rows, m - 1)
                to_rows(prod[:, m % 2, :], m % 2, o_tp)

            gated(swi2, b_hi, b_lo, both(lin1.hi, lin1.lo), lambda m: o_turn(m - 1) if m >= 1 else None,
                  lambda: pe.wait_ge(lin1.lo, KC - 1))
            o_turn(KC - 1)


def kernel(**inputs):
    import numpy as np
    import concourse.bacc as bacc
    from concourse.bass_utils import run_bass_kernel_spmd as run

    def units(w):
        w = np.asarray(w)
        return w.reshape(KC, P, -1, P).transpose(2, 1, 0, 3).reshape(-1, P, D)

    def pairs(a, b):
        return np.stack([units(a), units(b)], axis=1).reshape(-1, P, D)

    g = {k[3:]: np.asarray(v) for k, v in inputs.items() if k.startswith("L0_")}
    parts = [units(g["gnn_W"].T), units(g["ffn_lin0_w"]), pairs(g["ffn_swi1_w1"], g["ffn_swi1_w2"])]
    halves = []
    for h in range(2):
        c = slice(h * D, (h + 1) * D)
        halves.append([pairs(g["ffn_sh_w1"][:, c], g["ffn_sh_w3"][:, c]), units(g["ffn_sh_w2"][c, :])])
    parts += halves[0]
    for e in range(EXPERTS):
        parts += [pairs(g["ffn_exp_w1"][e], g["ffn_exp_w3"][e]), units(g["ffn_exp_w2"][e])]
    parts += halves[1]
    parts += [units(g["ffn_lin1_w"]), pairs(g["ffn_swi2_w1"], g["ffn_swi2_w2"])]
    biases = np.stack([g[n].reshape(KC, P) for n in (
        "ffn_lin0_b", "ffn_swi1_b1", "ffn_swi1_b2", "ffn_lin1_b", "ffn_swi2_b1", "ffn_swi2_b2")])
    arrays = {
        "x": np.ascontiguousarray(inputs["x"]),
        "src": np.ascontiguousarray(np.asarray(inputs["src"]).reshape(TT, EC)),
        "dst": np.ascontiguousarray(np.asarray(inputs["dst"]).reshape(TT, EC)),
        "gnn_b": np.ascontiguousarray(g["gnn_b"]),
        "biases": np.ascontiguousarray(biases.transpose(2, 0, 1)),
        "gate": np.pad(g["ffn_gate_w"].reshape(EXPERTS, KC, P).transpose(2, 1, 0),
                       ((0, 0), (0, 0), (0, P - EXPERTS))).reshape(P, D),
        "stream": np.concatenate(parts, axis=0),
    }
    nc = bacc.Bacc("TRN2", target_bir_lowering=False, num_devices=1)
    aps = {n: nc.dram_tensor(n + "_dram", a.shape, mybir.dt.from_np(a.dtype), kind="ExternalInput").ap()
           for n, a in arrays.items()}
    out = nc.dram_tensor("out_dram", (T, D), mybir.dt.float32, kind="ExternalOutput").ap()
    build(nc, out=out, **aps)
    r = run(nc, [{n + "_dram": a for n, a in arrays.items()}], core_ids=[0])
    return r.results[0]["out_dram"]
```
